# Optimizing a Trainium2 kernel written in Bass

```python
import numpy as np
import jax
import jax.numpy as jnp

def _softmax(x, axis=-1):
    return jax.nn.softmax(x, axis=axis)

def _gelu(x):
    return jax.nn.gelu(x, approximate=True)

def _silu(x):
    return jax.nn.silu(x)

def _sigmoid(x):
    return jax.nn.sigmoid(x)

def _layernorm(x, axis=-1, eps=1e-05):
    m = jnp.mean(x, axis=axis, keepdims=True)
    v = jnp.var(x, axis=axis, keepdims=True)
    return (x - m) / jnp.sqrt(v + eps)

def _scatter_add(tgt, idx, src, axis=0):
    return tgt.at[idx].add(src)

def _segment_sum(src, seg, n):
    return jax.ops.segment_sum(src, seg, n)
kernel_name = 'mk_gnn_preln_d1_gnn_r8_aa32a2'

def setup_inputs(seed: int=0):
    np.random.seed(seed)
    _w = jnp.asarray

    def _rec_inputs():
        import jax
        import jax.numpy as jnp
        _gk = jax.random.key(seed)
        x = -0.0008691 + 1 * jax.random.normal(jax.random.fold_in(_gk, 1), (12500, 128), jnp.float32)
        src = jax.random.randint(jax.random.fold_in(_gk, 2), (200000,), 0, 12500, jnp.int32)
        dst = jnp.minimum((12500 * jax.random.uniform(jax.random.fold_in(_gk, 3), (200000,)) ** 2.0).astype(jnp.int32), 99999)
        _o = jnp.argsort(dst, stable=True)
        src = src[_o]
        dst = dst[_o]
        edge_type_2 = jax.random.randint(jax.random.fold_in(_gk, 12), (200000,), 0, 2, jnp.int32)
        return (x, src, dst, edge_type_2)
    x, src, dst, edge_type_2 = _rec_inputs()

    def _L0_gnn_setup():
        import jax, jax.numpy as jnp
        import numpy as np
        IN_DIM = 128
        OUT_DIM = 128
        N_NODES = 1250
        N_EDGES = 80000
        key = jax.random.key(seed)
        ks = jax.random.split(key, 9)
        X = jax.random.normal(ks[0], (N_NODES, IN_DIM), dtype=jnp.float32)
        edge_index = jax.random.randint(ks[1], (2, N_EDGES), 0, N_NODES, dtype=jnp.int64)
        edge_types = jax.random.randint(ks[2], (N_EDGES,), 0, 2, dtype=jnp.int64)
        s = 1.0 / np.sqrt(IN_DIM)
        W_data = jax.random.uniform(ks[3], (OUT_DIM, IN_DIM), minval=-s, maxval=s, dtype=jnp.float32)
        b_data = jax.random.uniform(ks[4], (OUT_DIM,), minval=-s, maxval=s, dtype=jnp.float32)
        W_control = jax.random.uniform(ks[5], (OUT_DIM, IN_DIM), minval=-s, maxval=s, dtype=jnp.float32)
        b_control = jax.random.uniform(ks[6], (OUT_DIM,), minval=-s, maxval=s, dtype=jnp.float32)
        W_self = jax.random.uniform(ks[7], (OUT_DIM, IN_DIM), minval=-s, maxval=s, dtype=jnp.float32)
        b_self = jax.random.uniform(ks[8], (OUT_DIM,), minval=-s, maxval=s, dtype=jnp.float32)
        return {'X': X, 'edge_index': edge_index, 'edge_types': edge_types, 'W_data': W_data, 'b_data': b_data, 'W_control': W_control, 'b_control': b_control, 'W_self': W_self, 'b_self': b_self}
    _L0_gnn_all = _L0_gnn_setup()
    _L0_gnn_in = {k: v for k, v in _L0_gnn_all.items() if k in ('W_data', 'b_data', 'W_control', 'b_control', 'W_self', 'b_self')}
    del _L0_gnn_all
    return {'x': x, 'src': src, 'dst': dst, 'edge_type_2': edge_type_2, 'L0_gnn_W_data': _L0_gnn_in['W_data'], 'L0_gnn_b_data': _L0_gnn_in['b_data'], 'L0_gnn_W_control': _L0_gnn_in['W_control'], 'L0_gnn_b_control': _L0_gnn_in['b_control'], 'L0_gnn_W_self': _L0_gnn_in['W_self'], 'L0_gnn_b_self': _L0_gnn_in['b_self']}

def reference(x, src, dst, edge_type_2, L0_gnn_W_data, L0_gnn_b_data, L0_gnn_W_control, L0_gnn_b_control, L0_gnn_W_self, L0_gnn_b_self):
    import jax
    import jax.numpy as jnp

    def _L0_gnn_ref(X, edge_index, edge_types, W_data, b_data, W_control, b_control, W_self, b_self):
        import jax, jax.numpy as jnp
        import numpy as np
        IN_DIM = 128
        OUT_DIM = 128
        N_NODES = 1250
        N_EDGES = 80000
        src, dst = (edge_index[0], edge_index[1])
        Xs = X[src]
        m_data = Xs @ W_data.T + b_data
        m_ctrl = Xs @ W_control.T + b_control
        msg = jnp.where((edge_types == 0)[:, None], m_data, m_ctrl)
        agg = jax.ops.segment_sum(msg, dst, num_segments=X.shape[0])
        out = agg + (X @ W_self.T + b_self)
        return jax.nn.relu(out)
    edge_index = jnp.stack([src, dst])
    h = jnp.maximum(_layernorm(x, axis=-1), 0.0)
    x = x + _L0_gnn_ref(h, edge_index, edge_type_2, L0_gnn_W_data, L0_gnn_b_data, L0_gnn_W_control, L0_gnn_b_control, L0_gnn_W_self, L0_gnn_b_self)
    return x

_drawn_inputs = setup_inputs


def setup_inputs(seed=0):
    import zlib

    import numpy as np

    out = dict(_drawn_inputs(seed))
    spreads = {}
    factors = {'L0_gnn_b_self': 4.917}
    for name, (base, spread) in spreads.items():
        noise = np.random.default_rng([zlib.crc32(name.encode()), seed]).standard_normal(out[name].shape)
        drawn = base * np.exp(spread * noise) if base else spread * noise
        out[name] = jnp.asarray(drawn.astype(out[name].dtype))
    for name, factor in factors.items():
        out[name] = (out[name] * factor).astype(out[name].dtype)
    return out
```

```python
import concourse.bass as bass
from concourse import mybir
from contextlib import ExitStack
import numpy as np

F32 = mybir.dt.float32
I32 = mybir.dt.int32
ALU = mybir.AluOpType
ACT = mybir.ActivationFunctionType
AX_X = mybir.AxisListType.X

N, E, D, P = 12500, 200000, 128, 128
EPS = 1e-5
TILES = -(-N // P)
ROWS = TILES * P
TAIL = N - (TILES - 1) * P
CT = 7
CHUNKS = TILES // CT
Q = 4
GE = Q * P
BODY = 8
GROUPS = -(-(-(-E // GE)) // BODY) * BODY
GB = -(-GROUPS // P)
LISTS = GB * P
WIN = 128
WIDE = 512
SUMS = -(-(N + WIDE) // P) * P
FAR = 1.0e5
PIECES = -(-CT // 2)
ITERS = GROUPS // BODY
SLOTS = BODY // 2
AHEAD = 8
LEAD = 4
MORE_MOST = (N - 1 + WIDE - WIN) // WIDE
WIDE_MOST = GROUPS * (2 * MORE_MOST + 1)
assert CHUNKS * CT == TILES and CHUNKS % 2 == 0 and TILES == 2 * ITERS


def edge_parts(edges):
    full = E // (P * GE)
    at = full * P * GE
    some = (E - at) // GE
    end = at + some * GE
    parts = [(b, P, GE, edges[b * P * GE:(b + 1) * P * GE].rearrange("(p e) -> p e", e=GE)) for b in range(full)]
    parts.append((full, some, GE, edges[at:end].rearrange("(p e) -> p e", e=GE)))
    return parts, (full, some, E - end, edges[end:E].rearrange("(p e) -> p e", p=1))


def build(nc, x, src, dst, edge_type, w_data, b_data, w_control, b_control, w_self, b_self, out):
    ctx = ExitStack()
    with ctx:
        def sb(name, shape, dt=F32):
            return ctx.enter_context(nc.sbuf_tensor(name, shape, dt))

        def sem(name):
            return ctx.enter_context(nc.semaphore(name))

        table = nc.dram_tensor("message_table", (2 * ROWS, D), F32, kind="Internal").ap()

        ident = sb("ident", [P, P])
        ones = sb("ones", [P, P])
        iota = sb("iota", [P, WIDE])
        eps = sb("eps", [P, 1])
        w_rows = sb("w_rows", [P, 3, D])
        w_t = sb("w_t", [P, 3, D])
        bias_row = sb("bias_row", [1, 2, D])
        bias_all = sb("bias_all", [P, 2, D])
        bias_self = sb("bias_self", [P, 1])
        sums = sb("sums", [P, SUMS])
        lists = [sums[:, n * LISTS * Q:(n + 1) * LISTS * Q].rearrange("p (b e) -> p b e", b=GB) for n in range(5)]
        src_rows, dst_rows, type_rows = (r.bitcast(I32) for r in lists[0:3])
        idx_f, dst_f = lists[3:5]
        least = sb("least", [P, GB])
        most = sb("most", [P, GB])
        base_more = sb("base_more", [P, 2, GB])
        more_i = sb("more_i", [P, GB], I32)
        base_diag = sb("base_diag", [P, GB, P])
        base_all = sb("base_all", [P, LISTS])
        idx_cols = sb("idx_cols", [P, LISTS, Q])
        rel_cols = sb("rel_cols", [P, LISTS + 1, Q])
        steer = sb("steer", [1, 2, LISTS + 8], I32)
        xs = sb("xs", [P, TILES, D])
        stats = sb("stats", [P, 2, CT, 6])
        mean_var = sb("mean_var", [P, 2, CT, 2])
        std = sb("std", [P, 2, CT])
        rstd = sb("rstd", [P, 2, CT])
        shift = sb("shift", [P, 2, CT])
        h_and_msgs = sb("h_and_msgs", [P, 2 * CT * D * 3])
        h_t = sb("h_t", [P, 2, CT, D])
        h = h_and_msgs[:, 0:2 * CT * D].rearrange("p (b t d) -> p b t d", b=2, t=CT)
        msgs = h_and_msgs[:, 2 * CT * D:].rearrange("p (b t y d) -> p b t y d", b=2, t=CT, y=2)

        stage = sb("stage", [P, 2, BODY // 2 * Q], I32)
        onehot = sb("onehot", [P, 2, Q, WIN])
        rel_wide = sb("rel_wide", [P, Q])
        got = h_and_msgs[:, 0:SLOTS * Q * D].rearrange("p (s d) -> p s d", d=D)
        relu_sums = h_and_msgs[:, 0:2 * CT * D].rearrange("p (b c) -> p b c", b=2)
        onehot_wide = h_and_msgs[:, SLOTS * Q * D:SLOTS * Q * D + Q * WIDE].rearrange("p (q w) -> p q w", q=Q)

        bank = [ctx.enter_context(nc.psum_tensor(f"bank{n}", [P, 2, 512], F32)) for n in range(4)]
        edge_ps = [bank[0][:, 0, :], bank[0][:, 1, :]]
        steer_ps = [bank[1][0:1, 0, :], bank[1][0:1, 1, :]]
        base_ps = bank[2][:, 0, :]
        w_ps = bank[2][:, 1, :]
        bias_ps = bank[3][:, 0, 0:2 * D]
        self_ps = bank[2][:, :, :].rearrange("p a c -> p (a c)")[:, 0:CT * D]
        h_ps = bank[3][:, :, :].rearrange("p a c -> p (a c)")[:, 0:CT * D]
        msg_ps = [bank[n // 2][:, n % 2, :] for n in range(PIECES)]
        win_ps = [bank[0][:, 0, 0:WIN], bank[0][:, 1, 0:WIN]]
        wide_ps = bank[1][:, 0, :]
        out_ps = [bank[n][:, :, :].rearrange("p a c -> p (a c)")[:, 0:CT * D] for n in (2, 3)]

        weights_loaded = sem("weights_loaded")
        biases_loaded = sem("biases_loaded")
        src_loaded = sem("src_loaded")
        dst_loaded = sem("dst_loaded")
        type_loaded = sem("type_loaded")
        pads_set = sem("pads_set")
        consts_set = sem("consts_set")
        ident_zero = sem("ident_zero")
        w_in_psum = sem("w_in_psum")
        w_ready = sem("w_ready")
        dve_chain = sem("dve_chain")
        lists_ready = sem("lists_ready")
        steer_in_psum = sem("steer_in_psum")
        steer_ready = sem("steer_ready")
        base_in_psum = sem("base_in_psum")
        base_ready = sem("base_ready")
        cols_in_psum = sem("cols_in_psum")
        cols_copied = sem("cols_copied")
        x_tail_zero = sem("x_tail_zero")
        x_tail_loaded = sem("x_tail_loaded")
        x_loaded = [sem("x_loaded_even"), sem("x_loaded_odd")]
        moments_done = sem("moments_done")
        stats_ready = sem("stats_ready")
        rstd_done = sem("rstd_done")
        waits_passed = sem("waits_passed")
        slots_taken = sem("slots_taken")
        std_ready = sem("std_ready")
        norm_ready = sem("norm_ready")
        h_ready = sem("h_ready")
        h_t_in_psum = sem("h_t_in_psum")
        h_t_ready = sem("h_t_ready")
        msgs_in_psum = sem("msgs_in_psum")
        msgs_ready = sem("msgs_ready")
        msgs_stored = [sem("msgs_stored_even"), sem("msgs_stored_odd")]
        staged = sem("staged")
        got_landed = [sem(f"got_landed{s}") for s in range(BODY // 2)]
        onehot_ready = sem("onehot_ready")
        sums_in_psum = sem("sums_in_psum")
        groups_added = sem("groups_added")
        wide_chain = sem("wide_chain")
        wide_ready = sem("wide_ready")
        wide_in_psum = sem("wide_in_psum")
        self_in_psum = sem("self_in_psum")
        self_ready = sem("self_ready")
        total_in_psum = sem("total_in_psum")
        relu_ready = sem("relu_ready")
        out_ready = sem("out_ready")
        out_stored = [sem("out_stored_even"), sem("out_stored_odd")]

        block = ctx.enter_context(nc.Block())

        def x_view(dram, first, tiles):
            return dram[bass.ds(first * P, tiles * P), :].rearrange("(t p) d -> p t d", p=P)

        LIST_DMAS = len(edge_parts(src)[0]) + 1

        @block.sync
        def _(sp):
            sp.wait_ge(pads_set, 3)
            for rows, edges, loaded in ((dst_rows, dst, dst_loaded), (src_rows, src, src_loaded),
                                        (type_rows, edge_type, type_loaded)):
                parts, (b, g, n, rest) = edge_parts(edges)
                for blk, groups, ge, view in parts:
                    sp.dma_start(rows[0:groups, blk, :], view).then_inc(loaded, 16)
                sp.dma_start(rows[g:g + 1, b, 0:n], rest).then_inc(loaded, 16)
            for k in range(2):
                sp.dma_start(xs[:, k * CT:(k + 1) * CT, :], x_view(x, k * CT, CT)).then_inc(x_loaded[k], 16)
            with sp.Fori(1, CHUNKS // 2 - 1) as i:
                for b in range(2):
                    sp.wait_ge(x_loaded[b], 16 * i)
                    sp.dma_start(xs[:, bass.ds((2 * i + b) * CT, CT), :], x_view(x, (2 * i + b) * CT, CT))\
                      .then_inc(x_loaded[b], 16)
            for b in range(2):
                k = CHUNKS - 2 + b
                sp.wait_ge(x_loaded[b], 16 * (CHUNKS // 2 - 1))
                sp.dma_start(xs[:, k * CT:(k + 1) * CT - b, :], x_view(x, k * CT, CT - b)).then_inc(x_loaded[b], 16)

            with sp.Fori(0, CHUNKS // 2 - 1) as i:
                for b in range(2):
                    sp.wait_ge(out_ready, 2 * i + b + 1)
                    sp.dma_start(x_view(out, (2 * i + b) * CT, CT), xs[:, bass.ds((2 * i + b) * CT, CT), :])\
                      .then_inc(out_stored[b], 16)
            for b in range(2):
                k = CHUNKS - 2 + b
                sp.wait_ge(out_ready, k + 1)
                sp.dma_start(x_view(out, k * CT, CT - b), xs[:, k * CT:(k + 1) * CT - b, :]).then_inc(out_stored[b], 16)
            sp.dma_start(out[N - TAIL:N, :], xs[0:TAIL, TILES - 1, :]).then_inc(out_stored[0], 16)
            sp.wait_ge(out_stored[0], 16 * (CHUNKS // 2 + 1))
            sp.wait_ge(out_stored[1], 16 * (CHUNKS // 2))

        @block.gpsimd
        def _(pool):
            nc.gpsimd.memset(ident[:, :], 0.0).then_inc(ident_zero, 1)
            pool.wait_ge(ident_zero, 1)
            nc.gpsimd.affine_select(out=ident[:, :], in_=ident[:, :], compare_op=ALU.not_equal, fill=1.0, base=0,
                                    pattern=[[-1, P]], channel_multiplier=1).then_inc(consts_set, 1)
            nc.gpsimd.iota(iota[:, :], pattern=[[1, WIDE]], base=0, channel_multiplier=0,
                           allow_small_or_imprecise_dtypes=True).then_inc(consts_set, 1)

            def store(k, b):
                pool.wait_ge(msgs_ready, PIECES * (k + 1))
                for y in range(2):
                    pool.dma_start(table[bass.ds(k * CT * P + y * ROWS, CT * P), :]
                                   .rearrange("(t p) d -> p t d", p=P), msgs[:, b, :, y, :]).then_inc(msgs_stored[b], 16)

            with pool.Fori(0, CHUNKS // 2) as i:
                for b in range(2):
                    store(2 * i + b, b)

            for b in range(2):
                pool.wait_ge(msgs_stored[b], 32 * (CHUNKS // 2))

            with pool.Fori(0, ITERS) as i:
                for s in range(BODY):
                    half, slot = s // (BODY // 2), s % SLOTS
                    if s % (BODY // 2) == 0:
                        pool.wait_ge(staged, 2 * i + half + 1)
                    pool.wait_ge(groups_added, AHEAD + i * BODY + s - SLOTS + 2)
                    pool.sem_inc(slots_taken, 1)
                    for q in range(Q):
                        c = s % (BODY // 2) * Q + q
                        pool.indirect_dma_start(
                            out=got[:, slot * Q + q, :], out_offset=None, in_=table[:, :],
                            in_offset=bass.IndirectOffsetOnAxis(ap=stage[:, half, c:c + 1], axis=0)).then_inc(got_landed[slot], 16)

        @block.scalar
        def _(act):
            for n, w in enumerate((w_data, w_control, w_self)):
                act.dma_start(w_rows[:, n, :], w[:, :]).then_inc(weights_loaded, 16)
            for n, v in enumerate((b_data, b_control)):
                act.dma_start(bias_row[0:1, n, :], v.rearrange("(a d) -> a d", a=1)).then_inc(biases_loaded, 16)
            act.dma_start(bias_self[:, :], b_self.rearrange("(d a) -> d a", a=1)).then_inc(biases_loaded, 16)
            act.wait_ge(x_tail_zero, 1)
            act.dma_start(xs[0:TAIL, TILES - 1, :], x[N - TAIL:N, :]).then_inc(x_tail_loaded, 16)
            act.wait_ge(w_in_psum, 1)
            nc.scalar.copy(w_t[:, :, :].rearrange("p a d -> p (a d)"), w_ps[:, 0:3 * D]).then_inc(w_ready, 1)
            act.wait_ge(w_in_psum, 2)
            nc.scalar.copy(bias_all[:, :, :].rearrange("p a d -> p (a d)"), bias_ps).then_inc(w_ready, 1)

            for q in range(Q):
                act.wait_ge(cols_in_psum, 2 * q + 1)
                nc.scalar.copy(idx_cols[:, :, q], edge_ps[0]).then_inc(cols_copied, 1)

            def root(k, b):
                act.wait_ge(stats_ready, k + 1)
                nc.scalar.activation(std[:, b, :], mean_var[:, b, :, 1], ACT.Sqrt, bias=eps[:, 0:1])\
                  .then_inc(std_ready, 1)

            def normalise(k, b):
                act.wait_ge(norm_ready, k + 1)
                if positive(k - 1):
                    act.wait_ge(h_t_in_psum, k - 1)
                for j in range(CT):
                    ins = nc.scalar.activation(h[:, b, j, :], flat(xs[:, bass.ds(k * CT + j, 1), :]),
                                               ACT.Relu, bias=shift[:, b, j:j + 1], scale=rstd[:, b, j:j + 1])
                ins.then_inc(h_ready, 1)

            def copy_h_t(k, b):
                act.wait_ge(h_t_in_psum, k + 1)
                if positive(k - 1):
                    act.wait_ge(self_in_psum, k - 1)
                nc.scalar.copy(h_t[:, b, :, :].rearrange("p t d -> p (t d)"), h_ps).then_inc(h_t_ready, 1)

            def copy_self(k):
                act.wait_ge(self_in_psum, k + 1)
                nc.scalar.activation(sums[:, bass.ds(k * CT * P, CT * P)], self_ps, ACT.Identity,
                                     bias=bias_self[:, 0:1]).then_inc(self_ready, 1)

            act.wait_ge(consts_set, 3)
            act.wait_ge(biases_loaded, 48)
            act.wait_ge(cols_copied, 2 * Q)

            def step(k, b):
                if inside(k):
                    root(k, b)
                if inside(k - 1):
                    normalise(k - 1, 1 - b)
                if inside(k - 2):
                    copy_h_t(k - 2, b)
                if inside(k - 3):
                    copy_self(k - 3)

            steps(act, step)

            def stage_half(i, half):
                nc.scalar.copy(stage[:, half, :].rearrange("p (g q) -> p g q", q=Q),
                               idx_cols[:, bass.ds(i * BODY + half * (BODY // 2), BODY // 2), :]).then_inc(staged, 1)

            for half in range(2):
                stage_half(0, half)

            with act.Fori(1, ITERS) as i:
                for half in range(2):
                    for slot in range(SLOTS):
                        act.wait_ge(got_landed[slot], 16 * Q * (2 * i + half - 1))
                    stage_half(i, half)

            act.wait_ge(groups_added, AHEAD + 1 + GROUPS)

            def rectify(k, b):
                if positive(k - 1):
                    act.wait_ge(total_in_psum, k - 1)
                nc.scalar.activation(relu_sums[:, b, :], sums[:, bass.ds(k * CT * P, CT * P)], ACT.Relu)\
                  .then_inc(relu_ready, 1)

            rectify(0, 0)
            rectify(1, 1)
            with act.Fori(1, CHUNKS // 2) as i:
                for b in range(2):
                    rectify(2 * i + b, b)

        @block.vector
        def _(dve):
            chained = [0]

            def chain(ins):
                ins.then_inc(dve_chain, 1)
                chained[0] += 1
                dve.wait_ge(dve_chain, chained[0])

            for rows, pad in ((dst_rows, -1), (src_rows, 0), (type_rows, 0)):
                nc.vector.memset(rows[:, GB - 1, :], pad).then_inc(pads_set, 1)
            nc.vector.memset(xs[:, TILES - 1, :], 0.0).then_inc(x_tail_zero, 1)
            nc.vector.memset(ones[:, :], 1.0)
            nc.vector.memset(eps[:, :], EPS).then_inc(consts_set, 1)
            nc.vector.memset(steer[:, :, :], 0)
            nc.vector.memset(rel_cols[:, 0, :], 0.0)
            nc.vector.memset(sums[:, ROWS:SUMS], 0.0)

            dve.wait_ge(dst_loaded, 16 * LIST_DMAS)
            chain(nc.vector.tensor_copy(dst_f[:, :, :], dst_rows[:, :, :]))
            nc.vector.tensor_reduce(most[:, :], dst_f[:, :, :], AX_X, ALU.max)
            chain(nc.vector.tensor_scalar(idx_f[:, :, :], dst_f[:, :, :], 0.0, FAR, ALU.is_lt, ALU.mult))
            chain(nc.vector.tensor_tensor(idx_f[:, :, :], idx_f[:, :, :], dst_f[:, :, :], ALU.add))
            chain(nc.vector.tensor_reduce(least[:, :], idx_f[:, :, :], AX_X, ALU.min))
            chain(nc.vector.tensor_scalar(base_more[:, 0, :], least[:, :], float(N - 1), None, ALU.min))
            chain(nc.vector.tensor_tensor(most[:, :], most[:, :], base_more[:, 0, :], ALU.subtract))
            chain(nc.vector.tensor_scalar(more_i[:, :], most[:, :], float(WIDE - WIN), 0.0, ALU.add, ALU.max))
            chain(nc.vector.tensor_scalar(more_i[:, :], more_i[:, :], WIDE.bit_length() - 1, None, ALU.arith_shift_right))
            nc.vector.tensor_copy(base_more[:, 1, :], more_i[:, :])
            dve.wait_ge(consts_set, 3)
            for c in range(GB):
                ins = nc.vector.tensor_scalar(base_diag[:, c, :], ident[:, :], base_more[:, 0, c:c + 1], None, ALU.mult)
            dve.wait_ge(src_loaded, 16 * LIST_DMAS)
            dve.wait_ge(type_loaded, 16 * LIST_DMAS)
            chain(nc.vector.tensor_scalar(idx_f[:, :, :], type_rows[:, :, :], 0, float(ROWS), ALU.not_equal, ALU.mult))
            nc.vector.tensor_tensor(idx_f[:, :, :], idx_f[:, :, :], src_rows[:, :, :], ALU.add).then_inc(lists_ready, 1)

            dve.wait_ge(steer_in_psum, 1)
            for n in range(2):
                nc.vector.tensor_copy(steer[0:1, n, LEAD:LEAD + LISTS], steer_ps[n][0:1, 0:LISTS])\
                  .then_inc(steer_ready, 1)
            dve.wait_ge(base_in_psum, 1)
            chain(nc.vector.tensor_copy(base_all[:, :], base_ps[:, 0:LISTS]))
            for q in range(Q):
                dve.wait_ge(cols_in_psum, 2 * q + 2)
                nc.vector.tensor_tensor(rel_cols[:, 1:LISTS + 1, q], edge_ps[1], base_all[:, :], ALU.subtract)\
                  .then_inc(cols_copied, 1)

            def copy_h_t(k):
                dve.wait_ge(h_t_in_psum, k + 1)
                nc.vector.tensor_copy(h_t[:, bass.ds(k * CT, CT), :], h_ps.rearrange("p (t d) -> p t d", t=CT))\
                  .then_inc(h_t_ready, 1)

            def moments(k, b):
                dve.wait_ge(x_loaded[b], 16 * pair(k, b) + 16)
                for j in range(CT):
                    ins = nc.vector.bn_stats(stats[:, b, j, :], flat(xs[:, bass.ds(k * CT + j, 1), :]))
                ins.then_inc(moments_done, 1)
                dve.wait_ge(moments_done, k + 1)
                dve.sem_inc(waits_passed, 1)
                for j in range(CT):
                    ins = nc.vector.bn_aggr(mean_var[:, b, j, :], stats[:, b, j, :])
                ins.then_inc(stats_ready, 1)

            def scales(k, b):
                dve.wait_ge(std_ready, k + 1)
                if positive(k - 1):
                    dve.wait_ge(h_ready, k - 1)
                nc.vector.reciprocal(rstd[:, b, :], std[:, b, :]).then_inc(rstd_done, 1)
                dve.wait_ge(rstd_done, k + 1)
                nc.vector.scalar_tensor_tensor(out=shift[:, b, :], in0=mean_var[:, b, :, 0], scalar=-1.0,
                                               in1=rstd[:, b, :], op0=ALU.mult, op1=ALU.mult).then_inc(norm_ready, 1)

            def copy_messages(k, b):
                if positive(k - 1):
                    dve.wait_ge(msgs_stored[b], 32 * pair(k, b))
                for m in range(PIECES):
                    dve.wait_ge(msgs_in_psum, PIECES * k + m + 1)
                    n = min(2, CT - 2 * m)
                    nc.vector.tensor_tensor(msgs[:, b, 2 * m:2 * m + n, :, :].rearrange("p t y d -> p t (y d)"),
                                            msg_ps[m][:, 0:2 * D * n].rearrange("p (t c) -> p t c", t=n),
                                            bias_all[:, :, :].rearrange("p y d -> p (y d)").unsqueeze(1)
                                            .broadcast_to([P, n, 2 * D]), ALU.add).then_inc(msgs_ready, 1)

            def step(k, b):
                if inside(k):
                    moments(k, b)
                if inside(k - 1):
                    scales(k - 1, 1 - b)
                if inside(k - 3):
                    copy_messages(k - 3, 1 - b)

            dve.wait_ge(x_tail_loaded, 16)
            dve.wait_ge(w_ready, 2)
            steps(dve, step)

            dve.wait_ge(msgs_ready, PIECES * CHUNKS)
            dve.wait_ge(self_ready, CHUNKS)
            nc.vector.memset(win_ps[1], 0.0).then_inc(sums_in_psum, 1)
            nc.vector.memset(rel_wide[:, :], 0.0).then_inc(groups_added, AHEAD)
            links = nc.vector.alloc_register("links")
            windows = nc.vector.alloc_register("windows")
            wide_at = nc.vector.alloc_register("wide_at")
            nc.vector.reg_mov(links, 0)
            nc.vector.reg_mov(windows, 0)

            def link(ins):
                ins.then_inc(wide_chain, 1)
                nc.vector.reg_add(links, links, 1)
                dve.wait_ge(wide_chain, dve.snap(links, min_val=1, max_val=WIDE_MOST))

            def wide_windows(g, base, more):
                with dve.If(more > 0):
                    link(nc.vector.tensor_scalar(rel_wide[:, :], rel_of(g), float(WIN), None, ALU.subtract))
                    nc.vector.reg_mov(wide_at, base + WIN)
                    with dve.Fori(0, more) as _:
                        nc.vector.tensor_tensor(
                            onehot_wide, iota[:, :].unsqueeze(1).broadcast_to([P, Q, WIDE]),
                            rel_wide[:, :].unsqueeze(2).broadcast_to([P, Q, WIDE]), ALU.is_equal).then_inc(wide_ready, 1)
                        nc.vector.reg_add(windows, windows, 1)
                        dve.wait_ge(wide_in_psum, dve.snap(windows, min_val=1, max_val=WIDE_MOST))
                        at = sums[:, bass.ds(dve.snap(wide_at, min_val=WIN, max_val=N - 1), WIDE)]
                        link(nc.vector.tensor_tensor(at, at, wide_ps, ALU.add))
                        link(nc.vector.tensor_scalar(rel_wide[:, :], rel_wide[:, :], float(WIDE), None, ALU.subtract))
                        nc.vector.reg_add(wide_at, wide_at, WIDE)

            def rel_of(g):
                return rel_cols[:, bass.ds(g + 1, 1), :].rearrange("p a q -> p (a q)")

            def one_hot(g, buf):
                nc.vector.tensor_tensor(
                    onehot[:, buf, :, :], iota[:, 0:WIN].unsqueeze(1).broadcast_to([P, Q, WIN]),
                    rel_of(g).unsqueeze(2).broadcast_to([P, Q, WIN]),
                    ALU.is_equal).then_inc(onehot_ready, 1)

            def add_sums(g, base, buf):
                dve.wait_ge(sums_in_psum, g + 2)
                dve.wait_ge(groups_added, AHEAD + g + 1)
                at = sums[:, bass.ds(base, WIN)]
                nc.vector.tensor_tensor(at, at, win_ps[buf], ALU.add).then_inc(groups_added, 1)

            with dve.Fori(0, ITERS) as i:
                bases = load_steer(dve, nc, steer[0:1, 0, bass.ds(i * BODY + LEAD - 1, BODY + 1)], N - 1)
                mores = load_steer(dve, nc, steer[0:1, 1, bass.ds(i * BODY + LEAD - 1, BODY + 1)], MORE_MOST)
                for s in range(BODY):
                    one_hot(i * BODY + s, s % 2)
                    wide_windows(i * BODY + s - 1, bases[s], mores[s])
                    add_sums(i * BODY + s - 1, bases[s], (s + 1) % 2)
            last = GROUPS - 1
            base, = load_steer(dve, nc, steer[0:1, 0, LEAD + last:LEAD + last + 1], N - 1)
            more, = load_steer(dve, nc, steer[0:1, 1, LEAD + last:LEAD + last + 1], MORE_MOST)
            wide_windows(last, base, more)
            add_sums(last, base, 1)

            def finish(k, b):
                dve.wait_ge(total_in_psum, k + 1)
                xv = xs[:, bass.ds(k * CT, CT), :]
                nc.vector.tensor_tensor(xv, xv, out_ps[b].rearrange("p (t d) -> p t d", t=CT), ALU.add)\
                  .then_inc(out_ready, 1)

            with dve.Fori(0, CHUNKS // 2) as i:
                for b in range(2):
                    finish(2 * i + b, b)

        @block.tensor
        def _(pe):
            pe.wait_ge(consts_set, 3)
            pe.wait_ge(weights_loaded, 48)
            for n in range(3):
                ins = nc.tensor.transpose(w_ps[:, n * D:(n + 1) * D], w_rows[:, n, :], ident[:, :])
            ins.then_inc(w_in_psum, 1)
            pe.wait_ge(biases_loaded, 48)
            nc.tensor.matmul(bias_ps, ones[0:1, :], bias_row[0:1, :, :].rearrange("p y d -> p (y d)"),
                             start=True, stop=True).then_inc(w_in_psum, 1)

            pe.wait_ge(lists_ready, 1)
            for n in range(2):
                for c in range(GB):
                    ins = nc.tensor.matmul(steer_ps[n][0:1, c * P:(c + 1) * P], base_more[:, n, c:c + 1], ident[:, :],
                                           start=True, stop=True)
            ins.then_inc(steer_in_psum, 1)
            for c in range(GB):
                ins = nc.tensor.matmul(base_ps[:, c * P:(c + 1) * P], ones[:, :], base_diag[:, c, :],
                                       start=True, stop=True)
            ins.then_inc(base_in_psum, 1)
            for q in range(Q):
                for n, rows in enumerate((idx_f, dst_f)):
                    if q:
                        pe.wait_ge(cols_copied, 2 * q)
                    for c in range(GB):
                        ins = nc.tensor.transpose(edge_ps[n][:, c * P:(c + 1) * P], rows[:, c, q * P:(q + 1) * P],
                                                  ident[:, :])
                    ins.then_inc(cols_in_psum, 1)
            pe.wait_ge(cols_copied, 2 * Q)

            pe.wait_ge(w_ready, 2)

            def transposes(k, b):
                pe.wait_ge(h_ready, k + 1)
                if positive(k):
                    pe.wait_ge(h_t_ready, k)
                for j in range(CT):
                    ins = nc.tensor.transpose(h_ps[:, j * D:(j + 1) * D], h[:, b, j, :], ident[:, :])
                ins.then_inc(h_t_in_psum, 1)

            def products(k, b):
                pe.wait_ge(h_t_ready, k + 1)
                for j in range(CT):
                    if j % 2 == 0 and positive(k):
                        pe.wait_ge(msgs_ready, PIECES * (k - 1) + j // 2 + 1)
                    ins = nc.tensor.matmul(msg_ps[j // 2][:, j % 2 * 2 * D:(j % 2 + 1) * 2 * D], h_t[:, b, j, :],
                                           w_t[:, 0:2, :].rearrange("p y d -> p (y d)"), start=True, stop=True)
                    if j % 2 == 1 or j == CT - 1:
                        ins.then_inc(msgs_in_psum, 1)
                if positive(k):
                    pe.wait_ge(self_ready, k)
                for a, c in ((0, 4), (4, CT)):
                    ins = nc.tensor.matmul(self_ps[:, a * D:c * D], w_t[:, 2, :],
                                           h_t[:, b, a:c, :].rearrange("p t d -> p (t d)"), start=True, stop=True)
                ins.then_inc(self_in_psum, 1)

            def step(k, b):
                if inside(k - 1):
                    transposes(k - 1, 1 - b)
                if inside(k - 2):
                    products(k - 2, b)

            steps(pe, step)

            pe.wait_ge(msgs_ready, PIECES * CHUNKS)

            def group(g, i, s, more):
                slot, buf = s % SLOTS, s % 2
                pe.wait_ge(got_landed[slot], 16 * Q * ((BODY // SLOTS) * i + s // SLOTS + 1))
                pe.wait_ge(onehot_ready, g + 1)
                pe.wait_ge(groups_added, g + AHEAD)
                for q in range(Q):
                    ins = nc.tensor.matmul(win_ps[buf], got[:, slot * Q + q, :], onehot[:, buf, q, :],
                                           start=(q == 0), stop=(q == Q - 1))
                ins.then_inc(sums_in_psum, 1)
                with pe.If(more > 0):
                    with pe.Fori(0, more) as _:
                        nc.tensor.reg_add(windows, windows, 1)
                        pe.wait_ge(wide_ready, pe.snap(windows, min_val=1, max_val=WIDE_MOST))
                        for q in range(Q):
                            ins = nc.tensor.matmul(wide_ps, got[:, slot * Q + q, :], onehot_wide[:, q, :],
                                                   start=(q == 0), stop=(q == Q - 1))
                        ins.then_inc(wide_in_psum, 1)

            windows = nc.tensor.alloc_register("windows_pe")
            nc.tensor.reg_mov(windows, 0)

            pe.wait_ge(steer_ready, 2)
            with pe.Fori(0, ITERS) as i:
                mores = load_steer(pe, nc, steer[0:1, 1, bass.ds(i * BODY + LEAD, BODY)], MORE_MOST)
                for s in range(BODY):
                    group(i * BODY + s, i, s, mores[s])



            def totals(k, b):
                pe.wait_ge(relu_ready, k + 1)
                if positive(k - 1):
                    pe.wait_ge(out_ready, k - 1)
                for j in range(CT):
                    ins = nc.tensor.transpose(out_ps[b][:, j * D:(j + 1) * D], relu_sums[:, b, j * P:(j + 1) * P],
                                              ident[:, :])
                ins.then_inc(total_in_psum, 1)

            totals(0, 0)
            totals(1, 1)
            with pe.Fori(1, CHUNKS // 2) as i:
                for b in range(2):
                    totals(2 * i + b, b)


def positive(n):
    return not isinstance(n, int) or n > 0


def inside(k):
    return not isinstance(k, int) or 0 <= k < CHUNKS


def pair(k, b):
    return k // 2 if isinstance(k, int) else (k - b) // 2


def flat(ap):
    return ap.rearrange("p a d -> p (a d)")


def steps(eng, step):
    for k in range(4):
        step(k, k % 2)
    with eng.Fori(2, CHUNKS // 2) as i:
        for b in range(2):
            step(2 * i + b, b)
    for k in range(CHUNKS, CHUNKS + 3):
        step(k, k % 2)


def load_steer(eng, nc, entries, greatest):
    _, vals = nc.values_load_multi_w_load_instructions(
        entries, engines=[eng.engine], min_val=0, max_val=greatest,
        skip_runtime_bounds_check_because="the chip has clamped the bases to the nodes")
    return vals


INS = ["x", "src", "dst", "edge_type_2", "L0_gnn_W_data", "L0_gnn_b_data", "L0_gnn_W_control", "L0_gnn_b_control",
       "L0_gnn_W_self", "L0_gnn_b_self"]


def kernel(**inputs):
    import concourse.bacc as bacc
    from concourse.bass_utils import run_bass_kernel_spmd

    nc = bacc.Bacc("TRN2", target_bir_lowering=False, num_devices=1)
    arrays, args = {}, []
    for name in INS:
        a = np.ascontiguousarray(inputs[name])
        arrays[f"in_{name}"] = a
        args.append(nc.dram_tensor(f"in_{name}", a.shape, mybir.dt.from_np(a.dtype), kind="ExternalInput").ap())
    args.append(nc.dram_tensor("out", (N, D), F32, kind="ExternalOutput").ap())
    build(nc, *args)
    r = run_bass_kernel_spmd(nc, [arrays], core_ids=[0])
    return r.results[0]["out"]
```
